# Optimizing a Trainium2 kernel written in Bass

```python
import numpy as np
import jax
import jax.numpy as jnp

def _softmax(x, axis=-1):
    return jax.nn.softmax(x, axis=axis)

def _gelu(x):
    return jax.nn.gelu(x, approximate=True)

def _silu(x):
    return jax.nn.silu(x)

def _sigmoid(x):
    return jax.nn.sigmoid(x)

def _layernorm(x, axis=-1, eps=1e-05):
    m = jnp.mean(x, axis=axis, keepdims=True)
    v = jnp.var(x, axis=axis, keepdims=True)
    return (x - m) / jnp.sqrt(v + eps)

def _scatter_add(tgt, idx, src, axis=0):
    return tgt.at[idx].add(src)

def _segment_sum(src, seg, n):
    return jax.ops.segment_sum(src, seg, n)
kernel_name = 'mk_adj_preln_d1_adj_r2_30725a'

def setup_inputs(seed: int=0):
    np.random.seed(seed)
    _w = jnp.asarray

    def _rec_inputs():
        import jax
        import jax.numpy as jnp
        _gk = jax.random.key(seed)
        x = -0.0005207 + 1.001 * jax.random.normal(jax.random.fold_in(_gk, 1), (8192, 128), jnp.float32)
        _a = jax.random.bernoulli(jax.random.fold_in(_gk, 2), 0.00195312, (8192, 8192))
        _a = jnp.logical_or(_a, jnp.swapaxes(_a, -1, -2))
        _a = jnp.logical_or(_a, jnp.eye(8192, dtype=bool))
        _af = _a.astype(jnp.float32)
        _af = _af * jax.random.uniform(jax.random.fold_in(_gk, 3), (8192, 8192), jnp.float32, 0.05, 1)
        adj = _af
        return (x, adj)
    x, adj = _rec_inputs()

    def _L0_gnn_setup():
        import jax, jax.numpy as jnp
        import numpy as np
        ALPHA = 0.1
        N, F = (8192, 128)
        key = jax.random.key(seed)
        k1, k2, k3 = jax.random.split(key, 3)
        x = jax.random.normal(k1, (N, F), dtype=jnp.float32)
        adj = jax.random.uniform(k2, (N, N), dtype=jnp.float32)
        h = jax.random.normal(k3, (N, F), dtype=jnp.float32)
        return {'x': x, 'adj': adj, 'h': h}
    _L0_gnn_all = _L0_gnn_setup()
    _L0_gnn_in = {k: v for k, v in _L0_gnn_all.items() if k in ('h',)}
    del _L0_gnn_all
    return {'x': x, 'adj': adj, 'L0_gnn_h': _L0_gnn_in['h']}

def reference(x, adj, L0_gnn_h):
    import jax
    import jax.numpy as jnp

    def _L0_gnn_ref(x, adj, h):
        import jax, jax.numpy as jnp
        import numpy as np
        ALPHA = 0.1
        N, F = (8192, 128)
        return (1.0 - ALPHA) * (adj @ x) + ALPHA * h
    h = jnp.maximum(_layernorm(x, axis=-1), 0.0)
    x = x + _L0_gnn_ref(h, adj, L0_gnn_h)
    return x

_drawn_inputs = setup_inputs


def setup_inputs(seed=0):
    import zlib

    import numpy as np

    out = dict(_drawn_inputs(seed))
    spreads = {}
    factors = {'L0_gnn_h': 3.787}
    for name, (base, spread) in spreads.items():
        noise = np.random.default_rng([zlib.crc32(name.encode()), seed]).standard_normal(out[name].shape)
        drawn = base * np.exp(spread * noise) if base else spread * noise
        out[name] = jnp.asarray(drawn.astype(out[name].dtype))
    for name, factor in factors.items():
        out[name] = (out[name] * factor).astype(out[name].dtype)
    return out
```

```python
from contextlib import ExitStack

import concourse.bass as bass
from concourse import mybir

N, F = 8192, 128
P = 128
BLOCKS = N // P
CHUNK_BLOCKS = 4
COLS = CHUNK_BLOCKS * P
CHUNKS = BLOCKS // CHUNK_BLOCKS
PIECE_BLOCKS = 4
PIECES = BLOCKS // PIECE_BLOCKS
PIECE = PIECE_BLOCKS * COLS
RAW_SLOTS, HI_SLOTS, LO_SLOTS = 4, 4, 2
ALPHA = 0.1
EPS = 1e-5

GROUP_SIZES = [4, 12, 16, 16, 16]
GROUPS = [(sum(GROUP_SIZES[:g]), sum(GROUP_SIZES[:g + 1])) for g in range(len(GROUP_SIZES))]
GROUP_MAX = max(GROUP_SIZES)

LOAD_H0_AT = 4
STORE_AT = 8
COPY_X_AT = 6
TRANSPOSE_AT = 8
RESIDUAL_AT = 12
FINISH_AT = 1


def build(nc, x, adj, h0, out):
    fp32, fp32r = mybir.dt.float32, mybir.dt.float32r
    ALU = mybir.AluOpType
    ACT = mybir.ActivationFunctionType
    ctx = ExitStack()
    with ctx:
        def sb(name, shape, dt=fp32):
            return ctx.enter_context(nc.sbuf_tensor(name, shape, dt))

        def ps(name, shape):
            return ctx.enter_context(nc.psum_tensor(name, shape, fp32))

        def sem(name):
            return ctx.enter_context(nc.semaphore(name))

        x_sb = sb("x_sb", [P, BLOCKS, F])
        h_hi = sb("h_hi", [P, BLOCKS, F], fp32r)
        h_lo = sb("h_lo", [P, BLOCKS, F], fp32r)
        h_full = sb("h_full", [P, GROUP_MAX, F])
        raw = sb("raw", [P, RAW_SLOTS, PIECE])
        a_hi = sb("a_hi", [P, HI_SLOTS, PIECE], fp32r)
        a_lo = sb("a_lo", [P, LO_SLOTS, PIECE], fp32r)
        h0_sb = sb("h0_sb", [P, COLS])
        x_chunk = sb("x_chunk", [P, CHUNK_BLOCKS, F])
        residual = sb("residual", [P, COLS])
        finished = sb("finished", [P, COLS])
        ident = sb("ident", [P, P])
        stats = sb("stats", [P, BLOCKS, 6])
        mean_var = sb("mean_var", [P, BLOCKS, 2])
        var_eps = sb("var_eps", [P, BLOCKS])
        std = sb("std", [P, BLOCKS])
        rstd = sb("rstd", [P, BLOCKS])
        newton = sb("newton", [P, BLOCKS])
        shift = sb("shift", [P, BLOCKS])
        acc = ps("acc", [P, 2, COLS])
        x_t = ps("x_t", [P, COLS])

        x_landed = [sem(f"x_landed{g}") for g in range(len(GROUPS))]
        raw_landed = [sem(f"raw_landed{s}") for s in range(RAW_SLOTS)]
        h0_landed = sem("h0_landed")
        stored = sem("stored")
        ident_zero = sem("ident_zero")
        ident_ready = sem("ident_ready")
        var_ready = sem("var_ready")
        std_ready = sem("std_ready")
        scale_ready = sem("scale_ready")
        h_full_ready = sem("h_full_ready")
        h_hi_ready = sem("h_hi_ready")
        h_lo_ready = sem("h_lo_ready")
        hi_ready = sem("hi_ready")
        lo_ready = sem("lo_ready")
        piece_used = sem("piece_used")
        x_chunk_ready = sem("x_chunk_ready")
        x_t_ready = sem("x_t_ready")
        residual_ready = sem("residual_ready")
        finished_ready = sem("finished_ready")
        dve_step = sem("dve_step")

        x_v = x.rearrange("(p b) f -> p b f", b=BLOCKS)
        block = ctx.enter_context(nc.Block())

        @block.sync
        def _(sp):
            def load_piece(c, p):
                slot = p % RAW_SLOTS
                first = isinstance(c, int) and c == 0 and p < RAW_SLOTS
                if not first:
                    sp.wait_ge(lo_ready, c * PIECES + (p - RAW_SLOTS + 1))
                sp.dma_start(raw[:, slot, :], adj[c, p, :, :]).then_inc(raw_landed[slot], 16)

            def load_h0(c):
                if not (isinstance(c, int) and c == 0):
                    sp.wait_ge(residual_ready, c)
                sp.dma_start(h0_sb[:, :], h0[c, :, :]).then_inc(h0_landed, 16)

            def store(c, before):
                sp.wait_ge(finished_ready, c)
                sp.dma_start(out[before, :, :], finished[:, :]).then_inc(stored, 16)

            for p in range(PIECES):
                for g, (a, b) in enumerate(GROUPS):
                    if p == (0 if g == 0 else max(0, a // PIECE_BLOCKS - 3)):
                        sp.dma_start(x_sb[:, a:b, :], x_v[:, a:b, :]).then_inc(x_landed[g], 16)
                load_piece(0, p)
                if p == LOAD_H0_AT:
                    load_h0(0)
            with sp.Fori(1, CHUNKS) as c:
                for p in range(PIECES):
                    load_piece(c, p)
                    if p == LOAD_H0_AT:
                        load_h0(c)
                    if p == STORE_AT:
                        store(c, c - 1)
            store(CHUNKS, CHUNKS - 1)
            sp.wait_ge(stored, 16 * CHUNKS)

        @block.gpsimd
        def _(pool):
            nc.gpsimd.memset(ident[:, :], 0.0).then_inc(ident_zero, 1)
            pool.wait_ge(ident_zero, 1)
            nc.gpsimd.affine_select(out=ident[:, :], in_=ident[:, :], compare_op=ALU.not_equal, fill=1.0,
                                    base=0, pattern=[[-1, P]], channel_multiplier=1).then_inc(ident_ready, 1)

        @block.scalar
        def _(act):
            def round_piece(c, p):
                act.wait_ge(raw_landed[p % RAW_SLOTS],
                            16 * (c * (PIECES // RAW_SLOTS) + p // RAW_SLOTS + 1))
                if not (isinstance(c, int) and c == 0 and p < HI_SLOTS):
                    act.wait_ge(piece_used, c * PIECES + (p - HI_SLOTS + 1))
                nc.scalar.activation(a_hi[:, p % HI_SLOTS, :], raw[:, p % RAW_SLOTS, :],
                                     ACT.Copy).then_inc(hi_ready, 1)

            def root(g):
                a, b = GROUPS[g]
                act.wait_ge(var_ready, g + 1)
                nc.scalar.activation(std[:, a:b], var_eps[:, a:b], ACT.Sqrt).then_inc(std_ready, 1)

            def apply_norm(g):
                a, b = GROUPS[g]
                act.wait_ge(scale_ready, g + 1)
                if g:
                    act.wait_ge(h_lo_ready, g)
                for k in range(a, b):
                    last = nc.scalar.activation(h_full[:, k - a, :], x_sb[:, k, :], ACT.Relu,
                                                bias=shift[:, k:k + 1], scale=rstd[:, k:k + 1])
                last.then_inc(h_full_ready, 1)
                act.wait_ge(h_full_ready, g + 1)
                nc.scalar.activation(h_hi[:, a:b, :], h_full[:, 0:b - a, :], ACT.Copy).then_inc(h_hi_ready, 1)

            def copy_x(c):
                if not (isinstance(c, int) and c == 0):
                    act.wait_ge(x_t_ready, c)
                    act.wait_ge(residual_ready, c)
                blocks = slice(0, CHUNK_BLOCKS) if isinstance(c, int) else bass.ds(c * CHUNK_BLOCKS, CHUNK_BLOCKS)
                nc.scalar.activation(x_chunk[:, :, :], x_sb[:, blocks, :], ACT.Copy).then_inc(x_chunk_ready, 1)

            root(0)
            apply_norm(0)
            for p in range(PIECES):
                round_piece(0, p)
                if p == COPY_X_AT:
                    copy_x(0)
                for g, (a, b) in enumerate(GROUPS):
                    if g and p == max(0, a // PIECE_BLOCKS - 2):
                        root(g)
                        apply_norm(g)
            with act.Fori(1, CHUNKS) as c:
                for p in range(PIECES):
                    round_piece(c, p)
                    if p == COPY_X_AT:
                        copy_x(c)

        @block.vector
        def _(dve):
            steps = [0]

            def link(instruction):
                steps[0] += 1
                instruction.then_inc(dve_step, 1)
                dve.wait_ge(dve_step, steps[0])

            def statistics(g):
                a, b = GROUPS[g]
                dve.wait_ge(x_landed[g], 16)
                for k in range(a, b):
                    last = nc.vector.bn_stats(stats[:, k, :], x_sb[:, k, :])
                link(last)
                for k in range(a, b):
                    last = nc.vector.bn_aggr(mean_var[:, k, :], stats[:, k, :])
                link(last)
                v, r, n = var_eps[:, a:b], rstd[:, a:b], newton[:, a:b]
                nc.vector.tensor_scalar(v, mean_var[:, a:b, 1], EPS, None, ALU.add).then_inc(var_ready, 1)
                dve.wait_ge(std_ready, g + 1)
                link(nc.vector.reciprocal(r, std[:, a:b]))
                link(nc.vector.tensor_tensor(n, r, r, ALU.mult))
                link(nc.vector.tensor_tensor(n, n, v, ALU.mult))
                link(nc.vector.tensor_scalar(n, n, -0.5, 1.5, ALU.mult, ALU.add))
                link(nc.vector.tensor_tensor(r, r, n, ALU.mult))
                nc.vector.scalar_tensor_tensor(out=shift[:, a:b], in0=mean_var[:, a:b, 0], scalar=-1.0,
                                               in1=r, op0=ALU.mult, op1=ALU.mult).then_inc(scale_ready, 1)

            def h_low(g):
                a, b = GROUPS[g]
                dve.wait_ge(h_hi_ready, g + 1)
                nc.vector.tensor_tensor(h_lo[:, a:b, :], h_full[:, 0:b - a, :],
                                        h_hi[:, a:b, :].bitcast(fp32), ALU.subtract).then_inc(h_lo_ready, 1)

            def low_piece(c, p):
                dve.wait_ge(hi_ready, c * PIECES + (p + 1))
                if not (isinstance(c, int) and c == 0 and p < LO_SLOTS):
                    dve.wait_ge(piece_used, c * PIECES + (p - LO_SLOTS + 1))
                nc.vector.tensor_tensor(a_lo[:, p % LO_SLOTS, :], raw[:, p % RAW_SLOTS, :],
                                        a_hi[:, p % HI_SLOTS, :].bitcast(fp32),
                                        ALU.subtract).then_inc(lo_ready, 1)

            def add_residual(c):
                dve.wait_ge(h0_landed, 16 * c + 16)
                dve.wait_ge(x_t_ready, c + 1)
                if not (isinstance(c, int) and c == 0):
                    dve.wait_ge(finished_ready, c)
                nc.vector.scalar_tensor_tensor(out=residual[:, :], in0=h0_sb[:, :], scalar=ALPHA, in1=x_t[:, :],
                                               op0=ALU.mult, op1=ALU.add).then_inc(residual_ready, 1)

            def finish(c, bank):
                dve.wait_ge(piece_used, c * PIECES)
                dve.wait_ge(residual_ready, c)
                if not (isinstance(c, int) and c == 1):
                    dve.wait_ge(stored, 16 * c - 16)
                nc.vector.scalar_tensor_tensor(out=finished[:, :], in0=acc[:, bank, :], scalar=1.0 - ALPHA,
                                               in1=residual[:, :], op0=ALU.mult,
                                               op1=ALU.add).then_inc(finished_ready, 1)

            statistics(0)
            h_low(0)
            for p in range(PIECES):
                low_piece(0, p)
                for g, (a, b) in enumerate(GROUPS):
                    if g and p == max(0, a // PIECE_BLOCKS - 3):
                        statistics(g)
                    if g and p == max(0, a // PIECE_BLOCKS - 1):
                        h_low(g)
                if p == RESIDUAL_AT:
                    add_residual(0)

            def chunk(c, bank):
                for p in range(PIECES):
                    low_piece(c, p)
                    if p == FINISH_AT:
                        finish(c, 1 - bank)
                    if p == RESIDUAL_AT:
                        add_residual(c)

            with dve.Fori(0, CHUNKS // 2 - 1) as pair:
                chunk(pair * 2 + 1, 1)
                chunk(pair * 2 + 2, 0)
            chunk(CHUNKS - 1, 1)
            finish(CHUNKS, 1)

        @block.tensor
        def _(pe):
            def products(c, p, bank):
                hi, lo = a_hi[:, p % HI_SLOTS, :], a_lo[:, p % LO_SLOTS, :]
                blocks = [(p * PIECE_BLOCKS + i, slice(i * COLS, (i + 1) * COLS)) for i in range(PIECE_BLOCKS)]
                pe.wait_ge(hi_ready, c * PIECES + (p + 1))
                for k, cols in blocks:
                    nc.tensor.matmul(acc[:, bank, :], h_hi[:, k, :], hi[:, cols],
                                     start=(k == 0), stop=False)
                    nc.tensor.matmul(acc[:, bank, :], h_lo[:, k, :], hi[:, cols], start=False, stop=False)
                pe.wait_ge(lo_ready, c * PIECES + (p + 1))
                for k, cols in blocks:
                    last = nc.tensor.matmul(acc[:, bank, :], h_hi[:, k, :], lo[:, cols],
                                            start=False, stop=(k == BLOCKS - 1))
                last.then_inc(piece_used, 1)

            def transpose_x(c):
                pe.wait_ge(x_chunk_ready, c + 1)
                for j in range(CHUNK_BLOCKS):
                    last = nc.tensor.transpose(x_t[:, j * P:(j + 1) * P], x_chunk[:, j, :], ident[:, :])
                last.then_inc(x_t_ready, 1)

            pe.wait_ge(ident_ready, 1)
            with pe.Fori(0, CHUNKS // 2) as pair:
                for bank in range(2):
                    c = pair * 2 + bank
                    for p in range(PIECES):
                        k = p * PIECE_BLOCKS
                        g = [a for a, _ in GROUPS].index(k) if k in [a for a, _ in GROUPS] else None
                        if g is not None:
                            pe.wait_ge(x_landed[g], 16)
                            pe.wait_ge(h_lo_ready, g + 1)
                        products(c, p, bank)
                        if p == TRANSPOSE_AT:
                            transpose_x(c)


def kernel(x, adj, L0_gnn_h):
    import numpy as np
    import concourse.bacc as bacc
    from concourse.bass_utils import run_bass_kernel_spmd

    x, adj, h0 = np.asarray(x), np.asarray(adj), np.asarray(L0_gnn_h)
    adj_t = np.ascontiguousarray(
        adj.reshape(P, CHUNKS, CHUNK_BLOCKS, P, PIECES, PIECE_BLOCKS).transpose(1, 4, 3, 5, 2, 0)
    ).reshape(CHUNKS, PIECES, P, PIECE)
    h0_t = np.ascontiguousarray(
        h0.reshape(P, CHUNKS, CHUNK_BLOCKS, F).transpose(1, 3, 2, 0)).reshape(CHUNKS, F, COLS)
    arrays = {"x_dram": np.ascontiguousarray(x), "adj_dram": adj_t, "h0_dram": h0_t}

    nc = bacc.Bacc("TRN2", target_bir_lowering=False, num_devices=1)
    ins = [nc.dram_tensor(name, a.shape, mybir.dt.from_np(a.dtype), kind="ExternalInput").ap()
           for name, a in arrays.items()]
    out = nc.dram_tensor("out_dram", (CHUNKS, F, COLS), mybir.dt.float32, kind="ExternalOutput").ap()
    build(nc, *ins, out)
    result = run_bass_kernel_spmd(nc, [arrays], core_ids=[0]).results[0]["out_dram"]
    return np.ascontiguousarray(
        result.reshape(CHUNKS, F, CHUNK_BLOCKS, P).transpose(3, 0, 2, 1)).reshape(N, F)
```

```python
from contextlib import ExitStack

import concourse.bass as bass
from concourse import mybir

N, F = 8192, 128
P = 128
BLOCKS = N // P
CHUNK_BLOCKS = 4
COLS = CHUNK_BLOCKS * P
CHUNKS = BLOCKS // CHUNK_BLOCKS
PIECE_BLOCKS = 4
PIECES = BLOCKS // PIECE_BLOCKS
PIECE = PIECE_BLOCKS * COLS
ALPHA = 0.1
EPS = 1e-5

LOOP_CHUNKS = 3
LOOPS = (CHUNKS - 1) // LOOP_CHUNKS
LOOP_PIECES = LOOP_CHUNKS * PIECES
BANKS = 3
RAW_SLOTS, SPLIT_SLOTS = 6, 3
assert 1 + LOOPS * LOOP_CHUNKS == CHUNKS and LOOP_CHUNKS % BANKS == 0
assert LOOP_PIECES % RAW_SLOTS == 0 and LOOP_PIECES % SPLIT_SLOTS == 0

GROUP_SIZES = [4, 4, 8, 8, 16, 16, 8]
GROUPS = [(sum(GROUP_SIZES[:g]), sum(GROUP_SIZES[:g + 1])) for g in range(len(GROUP_SIZES))]
X_BEFORE_PIECE = {0: [0], 1: [1, 2], 2: [3], 3: [4], 4: [5], 5: [6]}

LOAD_H0_AT = 6
STORE_AT = 9
COPY_X_AT = 6
TRANSPOSE_AT = 8
RESIDUAL_AT = 12
FINISH_AT = 1


def build(nc, x, adj, h0, out):
    fp32, fp32r = mybir.dt.float32, mybir.dt.float32r
    ALU = mybir.AluOpType
    ACT = mybir.ActivationFunctionType
    ctx = ExitStack()
    with ctx:
        def sb(name, shape, dt=fp32):
            return ctx.enter_context(nc.sbuf_tensor(name, shape, dt))

        def ps(name, shape):
            return ctx.enter_context(nc.psum_tensor(name, shape, fp32))

        def sem(name):
            return ctx.enter_context(nc.semaphore(name))

        x_sb = sb("x_sb", [P, BLOCKS, F])
        h_hi = sb("h_hi", [P, BLOCKS, F], fp32r)
        h_lo = sb("h_lo", [P, BLOCKS, F], fp32r)
        raw = sb("raw", [P, RAW_SLOTS, PIECE])
        h0_sb = sb("h0_sb", [P, COLS])
        x_chunk = sb("x_chunk", [P, CHUNK_BLOCKS, F])
        residual = sb("residual", [P, COLS])
        finished = sb("finished", [P, COLS])
        ident = sb("ident", [P, P])
        stats = sb("stats", [P, BLOCKS, 6])
        mean_var = sb("mean_var", [P, BLOCKS, 2])
        var_eps = sb("var_eps", [P, BLOCKS])
        std = sb("std", [P, BLOCKS])
        rstd = sb("rstd", [P, BLOCKS])
        newton = sb("newton", [P, BLOCKS])
        shift = sb("shift", [P, BLOCKS])
        with nc.sbuf_tensor("h_full", [P, BLOCKS, F], fp32) as h_full:
            pass
        a_hi = sb("a_hi", [P, SPLIT_SLOTS, PIECE], fp32r)
        a_lo = sb("a_lo", [P, SPLIT_SLOTS, PIECE], fp32r)
        acc = ps("acc", [P, BANKS, COLS])
        x_t = ps("x_t", [P, COLS])

        x_landed = [sem(f"x_landed{g}") for g in range(len(GROUPS))]
        raw_landed = [sem(f"raw_landed{s}") for s in range(RAW_SLOTS)]
        h0_landed = sem("h0_landed")
        stored = sem("stored")
        ident_zero = sem("ident_zero")
        ident_ready = sem("ident_ready")
        var_ready = sem("var_ready")
        std_ready = sem("std_ready")
        scale_ready = sem("scale_ready")
        h_full_ready = sem("h_full_ready")
        h_hi_ready = sem("h_hi_ready")
        h_lo_ready = sem("h_lo_ready")
        hi_ready = sem("hi_ready")
        lo_ready = sem("lo_ready")
        piece_used = sem("piece_used")
        x_chunk_ready = sem("x_chunk_ready")
        x_t_ready = sem("x_t_ready")
        residual_ready = sem("residual_ready")
        finished_ready = sem("finished_ready")
        dve_step = sem("dve_step")

        def raw_slot(local):
            return local % RAW_SLOTS

        def raw_turn(i, local):
            return i * (LOOP_PIECES // RAW_SLOTS) + local // RAW_SLOTS

        def pieces_through(i, local):
            return i * LOOP_PIECES + (local + 1)

        def split_through(i, local):
            return i * LOOP_PIECES + (local + 1 - PIECES)

        def chunk_pieces(j):
            return [(p, j * PIECES + p) for p in range(PIECES)]

        x_v = x.rearrange("(p b) f -> p b f", b=BLOCKS)
        block = ctx.enter_context(nc.Block())

        @block.sync
        def _(sp):
            def load_piece(i, c, p, local):
                before = local - RAW_SLOTS
                if before >= PIECES:
                    sp.wait_ge(lo_ready, split_through(i, before))
                elif before >= 0:
                    sp.wait_ge(piece_used, pieces_through(i, before))
                sp.dma_start(raw[:, raw_slot(local), :],
                             adj[c, p, :, :]).then_inc(raw_landed[raw_slot(local)], 16)

            for p, local in chunk_pieces(0):
                for g in X_BEFORE_PIECE.get(p, []):
                    a, b = GROUPS[g]
                    sp.dma_start(x_sb[:, a:b, :], x_v[:, a:b, :]).then_inc(x_landed[g], 16)
                load_piece(0, 0, p, local)
                if p == LOAD_H0_AT:
                    sp.dma_start(h0_sb[:, :], h0[0, :, :]).then_inc(h0_landed, 16)
            with sp.Fori(0, LOOPS) as i:
                for j in range(1, LOOP_CHUNKS + 1):
                    c = i * LOOP_CHUNKS + j
                    for p, local in chunk_pieces(j):
                        load_piece(i, c, p, local)
                        if p == LOAD_H0_AT:
                            sp.wait_ge(residual_ready, c)
                            sp.dma_start(h0_sb[:, :], h0[c, :, :]).then_inc(h0_landed, 16)
                        if p == STORE_AT:
                            sp.wait_ge(finished_ready, c)
                            sp.dma_start(out[c - 1, :, :], finished[:, :]).then_inc(stored, 16)
            sp.wait_ge(finished_ready, CHUNKS)
            sp.dma_start(out[CHUNKS - 1, :, :], finished[:, :]).then_inc(stored, 16)
            sp.wait_ge(stored, 16 * CHUNKS)

        @block.gpsimd
        def _(pool):
            nc.gpsimd.memset(ident[:, :], 0.0).then_inc(ident_zero, 1)
            pool.wait_ge(ident_zero, 1)
            nc.gpsimd.affine_select(out=ident[:, :], in_=ident[:, :], compare_op=ALU.not_equal, fill=1.0,
                                    base=0, pattern=[[-1, P]], channel_multiplier=1).then_inc(ident_ready, 1)

        @block.scalar
        def _(act):
            def normalise(g):
                a, b = GROUPS[g]
                act.wait_ge(var_ready, g + 1)
                nc.scalar.activation(std[:, a:b], var_eps[:, a:b], ACT.Sqrt).then_inc(std_ready, 1)
                act.wait_ge(scale_ready, g + 1)
                for k in range(a, b):
                    last = nc.scalar.activation(h_full[:, k, :], x_sb[:, k, :], ACT.Relu,
                                                bias=shift[:, k:k + 1], scale=rstd[:, k:k + 1])
                last.then_inc(h_full_ready, 1)

            def high_h(g):
                a, b = GROUPS[g]
                act.wait_ge(h_full_ready, g + 1)
                nc.scalar.activation(h_hi[:, a:b, :], h_full[:, a:b, :], ACT.Copy).then_inc(h_hi_ready, 1)

            for g in range(len(GROUPS)):
                normalise(g)
                if g:
                    high_h(g - 1)
            high_h(len(GROUPS) - 1)
            nc.scalar.activation(x_chunk[:, :, :], x_sb[:, 0:CHUNK_BLOCKS, :], ACT.Copy).then_inc(x_chunk_ready, 1)
            act.wait_ge(h_lo_ready, len(GROUPS))
            with act.Fori(0, LOOPS) as i:
                for j in range(1, LOOP_CHUNKS + 1):
                    c = i * LOOP_CHUNKS + j
                    for p, local in chunk_pieces(j):
                        act.wait_ge(raw_landed[raw_slot(local)], raw_turn(i, local) * 16 + 16)
                        act.wait_ge(piece_used, pieces_through(i, local - SPLIT_SLOTS))
                        nc.scalar.activation(a_hi[:, local % SPLIT_SLOTS, :], raw[:, raw_slot(local), :],
                                             ACT.Copy).then_inc(hi_ready, 1)
                        if p == COPY_X_AT:
                            act.wait_ge(x_t_ready, c)
                            act.wait_ge(residual_ready, c)
                            nc.scalar.activation(x_chunk[:, :, :],
                                                 x_sb[:, bass.ds(c * CHUNK_BLOCKS, CHUNK_BLOCKS), :],
                                                 ACT.Copy).then_inc(x_chunk_ready, 1)

        @block.vector
        def _(dve):
            steps = [0]

            def link(instruction):
                steps[0] += 1
                instruction.then_inc(dve_step, 1)
                dve.wait_ge(dve_step, steps[0])

            def statistics(g):
                a, b = GROUPS[g]
                dve.wait_ge(x_landed[g], 16)
                for k in range(a, b):
                    last = nc.vector.bn_stats(stats[:, k, :], x_sb[:, k, :])
                link(last)
                for k in range(a, b):
                    last = nc.vector.bn_aggr(mean_var[:, k, :], stats[:, k, :])
                link(last)
                v, r, n = var_eps[:, a:b], rstd[:, a:b], newton[:, a:b]
                nc.vector.tensor_scalar(v, mean_var[:, a:b, 1], EPS, None, ALU.add).then_inc(var_ready, 1)
                dve.wait_ge(std_ready, g + 1)
                link(nc.vector.reciprocal(r, std[:, a:b]))
                link(nc.vector.tensor_tensor(n, r, r, ALU.mult))
                link(nc.vector.tensor_tensor(n, n, v, ALU.mult))
                link(nc.vector.tensor_scalar(n, n, -0.5, 1.5, ALU.mult, ALU.add))
                link(nc.vector.tensor_tensor(r, r, n, ALU.mult))
                nc.vector.scalar_tensor_tensor(out=shift[:, a:b], in0=mean_var[:, a:b, 0], scalar=-1.0,
                                               in1=r, op0=ALU.mult, op1=ALU.mult).then_inc(scale_ready, 1)

            def low_h(g):
                a, b = GROUPS[g]
                dve.wait_ge(h_hi_ready, g + 1)
                nc.vector.tensor_tensor(h_lo[:, a:b, :], h_full[:, a:b, :],
                                        h_hi[:, a:b, :].bitcast(fp32), ALU.subtract).then_inc(h_lo_ready, 1)

            def add_residual(c):
                dve.wait_ge(h0_landed, c * 16 + 16)
                dve.wait_ge(x_t_ready, c + 1)
                nc.vector.scalar_tensor_tensor(out=residual[:, :], in0=h0_sb[:, :], scalar=ALPHA, in1=x_t[:, :],
                                               op0=ALU.mult, op1=ALU.add).then_inc(residual_ready, 1)

            def finish(c, bank):
                dve.wait_ge(piece_used, c * PIECES)
                dve.wait_ge(residual_ready, c)
                nc.vector.scalar_tensor_tensor(out=finished[:, :], in0=acc[:, bank, :], scalar=1.0 - ALPHA,
                                               in1=residual[:, :], op0=ALU.mult,
                                               op1=ALU.add).then_inc(finished_ready, 1)

            for g in range(len(GROUPS)):
                statistics(g)
                if g >= 2:
                    low_h(g - 2)
            low_h(len(GROUPS) - 2)
            low_h(len(GROUPS) - 1)
            add_residual(0)
            with dve.Fori(0, LOOPS) as i:
                for j in range(1, LOOP_CHUNKS + 1):
                    c = i * LOOP_CHUNKS + j
                    for p, local in chunk_pieces(j):
                        dve.wait_ge(hi_ready, split_through(i, local))
                        dve.wait_ge(piece_used, pieces_through(i, local - SPLIT_SLOTS))
                        low = nc.vector.tensor_tensor(a_lo[:, local % SPLIT_SLOTS, :], raw[:, raw_slot(local), :],
                                                      a_hi[:, local % SPLIT_SLOTS, :].bitcast(fp32), ALU.subtract)
                        low.then_inc(lo_ready, 1)
                        if p == FINISH_AT:
                            finish(c, (j - 1) % BANKS)
                        if p == RESIDUAL_AT:
                            dve.wait_ge(finished_ready, c)
                            add_residual(c)
                            dve.wait_ge(stored, c * 16)
            finish(CHUNKS, (CHUNKS - 1) % BANKS)

        @block.tensor
        def _(pe):
            def transpose_x(c):
                pe.wait_ge(x_chunk_ready, c + 1)
                for j in range(CHUNK_BLOCKS):
                    last = nc.tensor.transpose(x_t[:, j * P:(j + 1) * P], x_chunk[:, j, :], ident[:, :])
                last.then_inc(x_t_ready, 1)

            group_of = {a // PIECE_BLOCKS: g for g, (a, _) in enumerate(GROUPS)}
            for p, local in chunk_pieces(0):
                if p in group_of:
                    pe.wait_ge(h_full_ready, group_of[p] + 1)
                pe.wait_ge(raw_landed[raw_slot(local)], 16 * raw_turn(0, local) + 16)
                for b in range(PIECE_BLOCKS):
                    k = p * PIECE_BLOCKS + b
                    last = nc.tensor.matmul(acc[:, 0, :], h_full[:, k, :],
                                            raw[:, raw_slot(local), b * COLS:(b + 1) * COLS],
                                            start=(k == 0), stop=(k == BLOCKS - 1))
                last.then_inc(piece_used, 1)
            pe.wait_ge(ident_ready, 1)
            transpose_x(0)
            pe.wait_ge(h_lo_ready, len(GROUPS))
            with pe.Fori(0, LOOPS) as i:
                for j in range(1, LOOP_CHUNKS + 1):
                    c = i * LOOP_CHUNKS + j
                    bank = acc[:, j % BANKS, :]
                    for p, local in chunk_pieces(j):
                        hi, lo = a_hi[:, local % SPLIT_SLOTS, :], a_lo[:, local % SPLIT_SLOTS, :]
                        blocks = [(p * PIECE_BLOCKS + b, slice(b * COLS, (b + 1) * COLS))
                                  for b in range(PIECE_BLOCKS)]
                        pe.wait_ge(hi_ready, split_through(i, local))
                        for k, cols in blocks:
                            nc.tensor.matmul(bank, h_hi[:, k, :], hi[:, cols], start=(k == 0), stop=False)
                            nc.tensor.matmul(bank, h_lo[:, k, :], hi[:, cols], start=False, stop=False)
                        pe.wait_ge(lo_ready, split_through(i, local))
                        for k, cols in blocks:
                            last = nc.tensor.matmul(bank, h_hi[:, k, :], lo[:, cols],
                                                    start=False, stop=(k == BLOCKS - 1))
                        last.then_inc(piece_used, 1)
                        if p == TRANSPOSE_AT:
                            transpose_x(c)


def kernel(x, adj, L0_gnn_h):
    import numpy as np
    import concourse.bacc as bacc
    from concourse.bass_utils import run_bass_kernel_spmd

    x, adj, h0 = np.asarray(x), np.asarray(adj), np.asarray(L0_gnn_h)
    adj_t = np.ascontiguousarray(
        adj.reshape(P, CHUNKS, CHUNK_BLOCKS, P, PIECES, PIECE_BLOCKS).transpose(1, 4, 3, 5, 2, 0)
    ).reshape(CHUNKS, PIECES, P, PIECE)
    h0_t = np.ascontiguousarray(
        h0.reshape(P, CHUNKS, CHUNK_BLOCKS, F).transpose(1, 3, 2, 0)).reshape(CHUNKS, F, COLS)
    arrays = {"x_dram": np.ascontiguousarray(x), "adj_dram": adj_t, "h0_dram": h0_t}

    nc = bacc.Bacc("TRN2", target_bir_lowering=False, num_devices=1)
    ins = [nc.dram_tensor(name, a.shape, mybir.dt.from_np(a.dtype), kind="ExternalInput").ap()
           for name, a in arrays.items()]
    out = nc.dram_tensor("out_dram", (CHUNKS, F, COLS), mybir.dt.float32, kind="ExternalOutput").ap()
    build(nc, *ins, out)
    result = run_bass_kernel_spmd(nc, [arrays], core_ids=[0]).results[0]["out_dram"]
    return np.ascontiguousarray(
        result.reshape(CHUNKS, F, CHUNK_BLOCKS, P).transpose(3, 0, 2, 1)).reshape(N, F)
```
